# Optimizing a Trainium2 kernel written in Bass

```python
import numpy as np
import jax
import jax.numpy as jnp

def _softmax(x, axis=-1):
    return jax.nn.softmax(x, axis=axis)

def _gelu(x):
    return jax.nn.gelu(x, approximate=True)

def _silu(x):
    return jax.nn.silu(x)

def _sigmoid(x):
    return jax.nn.sigmoid(x)

def _layernorm(x, axis=-1, eps=1e-05):
    m = jnp.mean(x, axis=axis, keepdims=True)
    v = jnp.var(x, axis=axis, keepdims=True)
    return (x - m) / jnp.sqrt(v + eps)

def _scatter_add(tgt, idx, src, axis=0):
    return tgt.at[idx].add(src)

def _segment_sum(src, seg, n):
    return jax.ops.segment_sum(src, seg, n)
kernel_name = 'mk_adj_preln_d1_adj_r2_53883b'

def setup_inputs(seed: int=0):
    np.random.seed(seed)
    _w = jnp.asarray

    def _rec_inputs():
        import jax
        import jax.numpy as jnp
        _gk = jax.random.key(seed)
        x = 8.953e-05 + 1 * jax.random.normal(jax.random.fold_in(_gk, 1), (5000, 64), jnp.float32)
        _w = (1.0 + jnp.arange(5000, dtype=jnp.float32)) ** (-0.5)
        _w = _w / _w.mean()
        _pij = jnp.clip(0.0032 * _w[:, None] * _w[None, :], 0.0, 1.0)
        _a = jax.random.uniform(jax.random.fold_in(_gk, 2), (5000, 5000)) < _pij
        _a = jnp.logical_or(_a, jnp.eye(5000, dtype=bool))
        _af = _a.astype(jnp.float32)
        _af = _af * jax.random.uniform(jax.random.fold_in(_gk, 3), (5000, 5000), jnp.float32, 0.05, 1)
        adj = _af
        return (x, adj)
    x, adj = _rec_inputs()

    def _L0_gnn_setup():
        import jax, jax.numpy as jnp
        import numpy as np
        N = 5000
        F = 64
        H = 64
        EPS = 1e-07
        key = jax.random.key(seed)
        k1, k2, k3, k4, k5 = jax.random.split(key, 5)
        x = jax.random.normal(k1, (N, F), dtype=jnp.float32)
        adj_matrix = jax.random.uniform(k2, (N, N), dtype=jnp.float32)
        num_neighbors = jax.random.uniform(k3, (N,), dtype=jnp.float32)
        fc_w = jax.random.normal(k4, (H, 2 * F), dtype=jnp.float32) / np.sqrt(2 * F)
        fc_b = jax.random.normal(k5, (H,), dtype=jnp.float32) * 0.01
        return {'x': x, 'adj_matrix': adj_matrix, 'num_neighbors': num_neighbors, 'fc_w': fc_w, 'fc_b': fc_b}
    _L0_gnn_all = _L0_gnn_setup()
    _L0_gnn_in = {k: v for k, v in _L0_gnn_all.items() if k in ('num_neighbors', 'fc_w', 'fc_b')}
    del _L0_gnn_all
    return {'x': x, 'adj': adj, 'L0_gnn_num_neighbors': _L0_gnn_in['num_neighbors'], 'L0_gnn_fc_w': _L0_gnn_in['fc_w'], 'L0_gnn_fc_b': _L0_gnn_in['fc_b']}

def reference(x, adj, L0_gnn_num_neighbors, L0_gnn_fc_w, L0_gnn_fc_b):
    import jax
    import jax.numpy as jnp

    def _L0_gnn_ref(x, adj_matrix, num_neighbors, fc_w, fc_b):
        import jax, jax.numpy as jnp
        import numpy as np
        N = 5000
        F = 64
        H = 64
        EPS = 1e-07
        neighbors = adj_matrix @ x
        neighbors = neighbors / (num_neighbors[:, None] + EPS)
        self_and_neighbor = jnp.concatenate([x, neighbors], axis=-1)
        out = self_and_neighbor @ fc_w.T + fc_b
        return jax.nn.relu(out)
    h = jnp.maximum(_layernorm(x, axis=-1), 0.0)
    x = x + _L0_gnn_ref(h, adj, L0_gnn_num_neighbors, L0_gnn_fc_w, L0_gnn_fc_b)
    return x

_drawn_inputs = setup_inputs


def setup_inputs(seed=0):
    import zlib

    import numpy as np

    out = dict(_drawn_inputs(seed))
    spreads = {}
    factors = {}
    for name, (base, spread) in spreads.items():
        noise = np.random.default_rng([zlib.crc32(name.encode()), seed]).standard_normal(out[name].shape)
        drawn = base * np.exp(spread * noise) if base else spread * noise
        out[name] = jnp.asarray(drawn.astype(out[name].dtype))
    for name, factor in factors.items():
        out[name] = (out[name] * factor).astype(out[name].dtype)
    return out
```

```python
from contextlib import ExitStack

import numpy as np

import concourse.bass as bass
from concourse import mybir

ALU = mybir.AluOpType
ACT = mybir.ActivationFunctionType
F32 = mybir.dt.float32
F32R = mybir.dt.float32r
AX_X = mybir.AxisListType.X

P = 128
BANK = 512
BANK_TILES = BANK // P
RAW = 6
SPLITS = RAW - 1
HALVES = 3
PEEL = 9
ROUND = 8
LN_EPS = 1e-5
DIV_EPS = 1e-7


def gnn_layer(nc, x, adj_t, num_neighbors, fc_t, fc_b, out):
    N, F = x.shape
    CH = N // P
    REM = N - CH * P
    TILES = CH + 1
    assert 0 < REM <= 32 and TILES % ROUND == 0 and (CH - PEEL) % RAW == 0 and 2 * F == P

    GROUPS = [(0, 16, 0), (16, 16, 4), (32, 8, 2)]
    G = len(GROUPS)
    assert sum(g[1] for g in GROUPS) == TILES
    WIDE = GROUPS[0][1] * P
    LOOPS = (CH - PEEL) // RAW

    def cols(g):
        t0, tiles, _ = GROUPS[g]
        return t0 * P, min(N, (t0 + tiles) * P) - t0 * P

    def banks(g):
        w = cols(g)[1]
        return [(GROUPS[g][2] + b, b * BANK, min(BANK, w - b * BANK)) for b in range(-(-w // BANK))]

    def split_index(q, s):
        return q * SPLITS + s

    def half_slot(s):
        return s % HALVES

    def half_slot_free(n, s):
        last = [s - d for d in range(1, RAW + 1) if (s - d) % RAW != SPLITS and half_slot((s - d) % RAW) == half_slot(s)][0]
        return n + (last - s) + 1

    with ExitStack() as ctx:
        def sb(name, shape, dt=F32):
            return ctx.enter_context(nc.sbuf_tensor(name, shape, dt))

        def sem(name):
            return ctx.enter_context(nc.semaphore(name))

        raw = [sb(f"raw{s}", [P, WIDE]) for s in range(RAW)]
        hi = [sb(f"hi{s}", [P, WIDE], F32R) for s in range(HALVES)]
        lo = [sb(f"lo{s}", [P, WIDE], F32R) for s in range(HALVES)]
        adj_rem = sb("adj_rem", [REM, WIDE])
        x_sb = sb("x_sb", [P, TILES, F])
        h_sb = sb("h_sb", [P, TILES, F])
        square = sb("square", [P, TILES, F])
        self_sb = sb("self_sb", [P, TILES, F])
        h_parts = sb("h_parts", [P, TILES, 2, F], F32R)
        w_split = [sb(f"w_split{s}", [P, 2 * F], F32R) for s in range(SPLITS)]
        w_plain = sb("w_plain", [P, 2 * F])
        w_rem = sb("w_rem", [REM, 2 * F])
        ht = [sb(f"ht{i}", [F + 1, ROUND * P]) for i in range(2)]
        sums = sb("sums", [P, WIDE])
        prod = sb("prod", [P, ROUND * F])
        w_self = sb("w_self", [F + 1, F])
        w_nbr = sb("w_nbr", [2 * F, F])
        nn = sb("nn", [P, TILES])
        rnn = sb("rnn", [P, TILES])
        ident = sb("ident", [P, P])
        mean = sb("mean", [P, TILES])
        var = sb("var", [P, TILES])
        std = sb("std", [P, TILES])
        rstd = sb("rstd", [P, TILES])

        psum = [ctx.enter_context(nc.psum_tensor(f"bank{b}", [P, BANK], F32)) for b in range(8)]
        T_BANKS, S_BANKS, Y_BANKS = (4, 5), (6, 7), (0, 1)

        x_cleared = sem("x_cleared")
        x_loaded = sem("x_loaded")
        nn_cleared = sem("nn_cleared")
        nn_loaded = sem("nn_loaded")
        weights_loaded = sem("weights_loaded")
        raw_loaded = [sem(f"raw_loaded{s}") for s in range(RAW)]
        rem_loaded = sem("rem_loaded")
        ln_dve = sem("ln_dve")
        ln_act = sem("ln_act")
        ident_cleared = sem("ident_cleared")
        ident_ready = sem("ident_ready")
        ones_ready = sem("ones_ready")
        h_hi_done = sem("h_hi_done")
        h_lo_done = sem("h_lo_done")
        plain_cleared = sem("plain_cleared")
        rem_ready = sem("rem_ready")
        staged = sem("staged")
        hi_done = sem("hi_done")
        lo_done = sem("lo_done")
        pe_done = sem("pe_done")
        rem_done = sem("rem_done")
        ht_transposed = sem("ht_transposed")
        ht_copied = sem("ht_copied")
        self_summed = sem("self_summed")
        self_copied = sem("self_copied")
        sums_copied = sem("sums_copied")
        y_ready = sem("y_ready")
        combine = sem("combine")
        out_ready = sem("out_ready")
        stored = sem("stored")
        rnn_chain = sem("rnn_chain")

        LN_STEPS = 7

        x_main = x[0:CH * P, :].rearrange("(p t) f -> p t f", t=CH)
        nn_main = num_neighbors[0:CH * P].rearrange("(p t) -> p t", t=CH)
        nn_rem = num_neighbors[CH * P:N].rearrange("(p t) -> p t", t=1)
        out_main = out[0:CH * P, :].rearrange("(p t) f -> p t f", t=CH)
        bias_row = fc_b.rearrange("(a f) -> a f", a=1)

        def bcast(v):
            return v.unsqueeze(2).to_broadcast([P, v.shape[1], F])

        def steps(eng, g, step, between=None):
            for c in range(PEEL):
                n = g * CH + c
                step(c, n, n // RAW, n % RAW)
                if between is not None:
                    between(c)
            with eng.Fori(0, LOOPS) as it:
                for j in range(RAW):
                    c0 = PEEL + j
                    n0 = g * CH + c0
                    step(it * RAW + c0, it * RAW + n0, it + n0 // RAW, n0 % RAW)

        def started(n, back):
            return not isinstance(n, int) or n >= back

        block = ctx.enter_context(nc.Block())

        @block.sync
        def _(sp):
            def load(g):
                c0, w = cols(g)

                def step(c, n, q, s):
                    if started(n, RAW):
                        if s < SPLITS:
                            sp.wait_ge(lo_done, split_index(q - 1, s) + 1)
                        else:
                            sp.wait_ge(pe_done, n - RAW + 1)
                    k0 = c * P
                    sp.dma_start(raw[s][:, 0:w], adj_t[bass.ds(k0, P), c0:c0 + w]).then_inc(raw_loaded[s], 16)
                return step

            def load_rem(g):
                c0, w = cols(g)
                if g:
                    sp.wait_ge(rem_done, g)
                sp.dma_start(adj_rem[:, 0:w], adj_t[CH * P:N, c0:c0 + w]).then_inc(rem_loaded, 16)

            def store(t0, t1):
                n_rows = min(t1, CH) - t0
                sp.dma_start(out_main[:, t0:t0 + n_rows, :], self_sb[:, t0:t0 + n_rows, :]).then_inc(stored, 16)

            for g in range(G):
                load_rem(g)
                steps(sp, g, load(g))
                if g:
                    t0, tiles, _ = GROUPS[g - 1]
                    sp.wait_ge(out_ready, (t0 + tiles) // ROUND)
                    store(t0, t0 + tiles)
            t0, tiles, _ = GROUPS[G - 1]
            sp.wait_ge(out_ready, TILES // ROUND)
            store(t0, t0 + tiles)
            sp.dma_start(out[CH * P:N, :], self_sb[0:REM, CH, :]).then_inc(stored, 16)
            sp.wait_ge(stored, 16 * (G + 1))

        @block.gpsimd
        def _(pool):
            nc.gpsimd.memset(ident[:], 0.0).then_inc(ident_cleared, 1)
            pool.wait_ge(ident_cleared, 1)
            nc.gpsimd.affine_select(out=ident[:], in_=ident[:], compare_op=ALU.not_equal, fill=1.0, base=0,
                                    pattern=[[-1, P]], channel_multiplier=1).then_inc(ident_ready, 1)
            pool.wait_ge(plain_cleared, 2)
            pool.wait_ge(ln_dve, LN_STEPS)
            nc.gpsimd.tensor_copy(w_rem[:, 0:F], h_sb[0:REM, CH, :]).then_inc(rem_ready, 1)
            pool.wait_ge(h_hi_done, 1)
            pool.wait_ge(h_lo_done, 1)

            def step(c, n, q, s):
                if started(n, RAW):
                    pool.wait_ge(pe_done, n - RAW + 1)
                if s < SPLITS:
                    nc.gpsimd.tensor_copy(w_split[s][:].rearrange("p (a b f) -> p a b f", a=1, b=2),
                                          h_parts[:, bass.ds(c, 1), :, :]).then_inc(staged, 1)
                else:
                    nc.gpsimd.tensor_copy(w_plain[:, 0:F].rearrange("p (a f) -> p a f", a=1),
                                          h_sb[:, bass.ds(c, 1), :]).then_inc(staged, 1)

            for g in range(G):
                steps(pool, g, step)

        @block.scalar
        def _(act):
            act.wait_ge(x_cleared, 1)
            act.dma_start(x_sb[:, 0:CH, :], x_main).then_inc(x_loaded, 16)
            act.dma_start(x_sb[0:REM, CH, :], x[CH * P:N, :]).then_inc(x_loaded, 16)
            act.wait_ge(nn_cleared, 1)
            act.dma_start(nn[:, 0:CH], nn_main).then_inc(nn_loaded, 16)
            act.dma_start(nn[0:REM, CH:TILES], nn_rem).then_inc(nn_loaded, 16)
            act.dma_start(w_self[0:F, :], fc_t[0:F, :]).then_inc(weights_loaded, 16)
            act.dma_start(w_self[F:F + 1, :], bias_row).then_inc(weights_loaded, 16)
            act.dma_start(w_nbr[0:F, :], fc_t[F:2 * F, :]).then_inc(weights_loaded, 16)
            act.dma_start(w_nbr[F:2 * F, :], fc_t[F:2 * F, :]).then_inc(weights_loaded, 16)

            def high(g):
                w = cols(g)[1]

                def step(c, n, q, s):
                    if s == SPLITS:
                        return
                    act.wait_ge(raw_loaded[s], 16 * q + 16)
                    free = half_slot_free(n, s)
                    if not isinstance(free, int) or free > 0:
                        act.wait_ge(pe_done, free)
                    nc.scalar.activation(hi[half_slot(s)][:, 0:w], raw[s][:, 0:w], ACT.Copy).then_inc(hi_done, 1)
                return step

            def ln_square():
                act.wait_ge(ln_dve, 2)
                nc.scalar.activation(square[:], h_sb[:], ACT.Square).then_inc(ln_act, 1)

            def ln_std():
                act.wait_ge(ln_dve, 4)
                nc.scalar.activation(std[:], var[:], ACT.Sqrt).then_inc(ln_act, 1)

            def split_h():
                act.wait_ge(ln_dve, LN_STEPS)
                nc.scalar.activation(h_parts[:, :, 0, :], h_sb[:], ACT.Copy).then_inc(h_hi_done, 1)

            def copy_ht(r):
                for i, b in enumerate(T_BANKS):
                    act.wait_ge(ht_transposed, 2 * r + i + 1)
                    if r >= 2 and i == 0:
                        act.wait_ge(self_summed, r - 1)
                    nc.scalar.activation(ht[r % 2][0:F, i * BANK:(i + 1) * BANK], psum[b][0:F, :],
                                         ACT.Copy).then_inc(ht_copied, 1)

            def copy_sums(g):
                act.wait_ge(rem_done, g + 1)
                if g:
                    act.wait_ge(y_ready, (GROUPS[g - 1][0] + GROUPS[g - 1][1]) // ROUND)
                for b, c0, w in banks(g):
                    nc.scalar.activation(sums[:, c0:c0 + w], psum[b][:, 0:w], ACT.Copy).then_inc(sums_copied, 1)

            ln_square()
            ln_std()
            for g in range(G):
                def between(c, g=g):
                    if g == 0 and c == 0:
                        split_h()
                    if g == 0 and c < TILES // ROUND:
                        copy_ht(c)
                    if g and c == 1:
                        copy_sums(g - 1)
                steps(act, g, high(g), between)
            copy_sums(G - 1)

        @block.vector
        def _(dve):
            nc.vector.memset(x_sb[:, CH, :], 0.0).then_inc(x_cleared, 1)
            nc.vector.memset(nn[:], 1.0).then_inc(nn_cleared, 1)
            for i in range(2):
                nc.vector.memset(ht[i][F:F + 1, :], 1.0).then_inc(ones_ready, 1)
            nc.vector.memset(w_plain[:], 0.0).then_inc(plain_cleared, 1)
            nc.vector.memset(w_rem[:], 0.0).then_inc(plain_cleared, 1)
            dve.wait_ge(x_cleared, 1)
            dve.wait_ge(x_loaded, 32)
            nc.vector.tensor_reduce(mean[:], x_sb[:], AX_X, ALU.add).then_inc(rnn_chain, 1)
            dve.wait_ge(rnn_chain, 1)
            nc.vector.tensor_scalar(mean[:], mean[:], 1.0 / F, None, ALU.mult).then_inc(ln_dve, 1)
            dve.wait_ge(ln_dve, 1)
            nc.vector.tensor_tensor(h_sb[:], x_sb[:], bcast(mean[:]), ALU.subtract).then_inc(ln_dve, 1)
            dve.wait_ge(ln_act, 1)
            nc.vector.tensor_reduce(var[:], square[:], AX_X, ALU.add).then_inc(ln_dve, 1)
            dve.wait_ge(ln_dve, 3)
            nc.vector.tensor_scalar(var[:], var[:], 1.0 / F, LN_EPS, ALU.mult, ALU.add).then_inc(ln_dve, 1)
            dve.wait_ge(ln_act, 2)
            nc.vector.reciprocal(rstd[:], std[:]).then_inc(ln_dve, 1)
            dve.wait_ge(ln_dve, 5)
            nc.vector.tensor_tensor(h_sb[:], h_sb[:], bcast(rstd[:]), ALU.mult).then_inc(ln_dve, 1)
            dve.wait_ge(ln_dve, 6)
            nc.vector.tensor_scalar(h_sb[:], h_sb[:], 0.0, None, ALU.max).then_inc(ln_dve, 1)
            dve.wait_ge(h_hi_done, 1)
            nc.vector.tensor_tensor(h_parts[:, :, 1, :], h_sb[:], h_parts[:, :, 0, :].bitcast(F32),
                                    ALU.subtract).then_inc(h_lo_done, 1)
            dve.wait_ge(nn_loaded, 32)
            nc.vector.tensor_scalar(nn[:], nn[:], DIV_EPS, None, ALU.add).then_inc(rnn_chain, 1)
            dve.wait_ge(rnn_chain, 2)
            nc.vector.reciprocal(rnn[:], nn[:]).then_inc(rnn_chain, 1)

            def low(g):
                w = cols(g)[1]

                def step(c, n, q, s):
                    if s == SPLITS:
                        return
                    dve.wait_ge(hi_done, split_index(q, s) + 1)
                    i = half_slot(s)
                    nc.vector.tensor_tensor(lo[i][:, 0:w], raw[s][:, 0:w], hi[i][:, 0:w].bitcast(F32),
                                            ALU.subtract).then_inc(lo_done, 1)
                return step

            def copy_self(r):
                dve.wait_ge(self_summed, r + 1)
                nc.vector.tensor_copy(self_sb[:, r * ROUND:(r + 1) * ROUND, :],
                                      psum[S_BANKS[r % 2]][:].rearrange("p (t f) -> p t f", f=F)).then_inc(self_copied, 1)

            def finish(r):
                t = slice(r * ROUND, (r + 1) * ROUND)
                p3 = prod[:].rearrange("p (t f) -> p t f", f=F)
                dve.wait_ge(y_ready, r + 1)
                if r == 0:
                    dve.wait_ge(rnn_chain, 3)
                nc.vector.tensor_tensor(p3, psum[Y_BANKS[r % 2]][:].rearrange("p (t f) -> p t f", f=F),
                                        bcast(rnn[:, t]), ALU.mult).then_inc(combine, 1)
                dve.wait_ge(combine, 2 * r + 1)
                dve.wait_ge(self_copied, TILES // ROUND)
                nc.vector.tensor_tensor(self_sb[:, t, :], p3, self_sb[:, t, :], ALU.add).then_inc(combine, 1)
                dve.wait_ge(combine, 2 * r + 2)
                nc.vector.scalar_tensor_tensor(self_sb[:, t, :], self_sb[:, t, :], 0.0, x_sb[:, t, :],
                                               ALU.max, ALU.add).then_inc(out_ready, 1)

            for g in range(G):
                def between(c, g=g):
                    if g == 0 and 1 <= c <= TILES // ROUND:
                        copy_self(c - 1)
                    if g and c in (4, 6):
                        finish(GROUPS[g - 1][0] // ROUND + (c - 4) // 2)
                steps(dve, g, low(g), between)
            finish(GROUPS[G - 1][0] // ROUND)

        @block.tensor
        def _(pe):
            def transpose_h(r):
                for i in range(ROUND):
                    t = r * ROUND + i
                    b = T_BANKS[i // BANK_TILES]
                    if r and i == 0:
                        pe.wait_ge(ht_copied, 2 * r)
                    last = nc.tensor.transpose(psum[b][0:F, (i % BANK_TILES) * P:(i % BANK_TILES + 1) * P],
                                               h_sb[:, t, :], ident[:])
                    if i % BANK_TILES == BANK_TILES - 1:
                        last.then_inc(ht_transposed, 1)

            def self_part(r):
                pe.wait_ge(ht_copied, 2 * (r + 1))
                if r >= 2:
                    pe.wait_ge(self_copied, r - 1)
                for i in range(ROUND):
                    last = nc.tensor.matmul(psum[S_BANKS[r % 2]][:, i * F:(i + 1) * F],
                                            ht[r % 2][:, i * P:(i + 1) * P], w_self[:], start=True, stop=True)
                last.then_inc(self_summed, 1)

            def neighbor_part(r, g):
                i0 = r * ROUND - GROUPS[g][0]
                before = sum(len(banks(k)) for k in range(g))
                pe.wait_ge(sums_copied, before + min(len(banks(g)), -(-(i0 + ROUND) // BANK_TILES)))
                if r >= 2:
                    pe.wait_ge(combine, 2 * (r - 2) + 1)
                for i in range(ROUND):
                    last = nc.tensor.matmul(psum[Y_BANKS[r % 2]][:, i * F:(i + 1) * F],
                                            sums[:, (i0 + i) * P:(i0 + i + 1) * P], w_nbr[:], start=True, stop=True)
                last.then_inc(y_ready, 1)

            def remainder(g):
                pe.wait_ge(rem_loaded, 16 * (g + 1))
                for b, c0, w in banks(g):
                    last = nc.tensor.matmul(psum[b][:, 0:w], w_rem[:], adj_rem[:, c0:c0 + w], start=False, stop=True)
                last.then_inc(rem_done, 1)

            def multiply(g):
                def step(c, n, q, s):
                    first = isinstance(c, int) and c == 0
                    pe.wait_ge(staged, n + 1)
                    if s < SPLITS:
                        i = half_slot(s)
                        pe.wait_ge(hi_done, split_index(q, s) + 1)
                        for b, c0, w in banks(g):
                            nc.tensor.matmul(psum[b][:, 0:w], w_split[s][:], hi[i][:, c0:c0 + w],
                                             start=first, stop=False)
                        pe.wait_ge(lo_done, split_index(q, s) + 1)
                        for b, c0, w in banks(g):
                            last = nc.tensor.matmul(psum[b][:, 0:w], w_split[s][:], lo[i][:, c0:c0 + w],
                                                    start=False, stop=False)
                    else:
                        pe.wait_ge(raw_loaded[s], 16 * q + 16)
                        for b, c0, w in banks(g):
                            last = nc.tensor.matmul(psum[b][:, 0:w], w_plain[:], raw[s][:, c0:c0 + w],
                                                    start=first, stop=False)
                    last.then_inc(pe_done, 1)
                return step

            pe.wait_ge(ident_ready, 1)
            pe.wait_ge(ln_dve, LN_STEPS)
            transpose_h(0)
            pe.wait_ge(ones_ready, 2)
            pe.wait_ge(weights_loaded, 64)
            pe.wait_ge(rem_ready, 1)
            for g in range(G):
                if g == 1:
                    pe.wait_ge(self_copied, TILES // ROUND)
                if g == 2:
                    pe.wait_ge(sums_copied, len(banks(0)))

                def between(c, g=g):
                    if g == 0 and c < TILES // ROUND:
                        self_part(c)
                        if c + 1 < TILES // ROUND:
                            transpose_h(c + 1)
                    if g and c in (2, 4):
                        neighbor_part(GROUPS[g - 1][0] // ROUND + (c - 2) // 2, g - 1)
                steps(pe, g, multiply(g), between)
                remainder(g)
            neighbor_part(GROUPS[G - 1][0] // ROUND, G - 1)


def kernel(x, adj, L0_gnn_num_neighbors, L0_gnn_fc_w, L0_gnn_fc_b):
    import concourse.bacc as _bacc
    from concourse.bass_utils import run_bass_kernel_spmd as _run

    x = np.ascontiguousarray(x)
    n, f = x.shape
    whole = n // P * P
    order = np.concatenate([np.arange(whole).reshape(P, whole // P).T.ravel(), np.arange(whole, n)])
    arrays = {
        "x": x,
        "adj_t": np.ascontiguousarray(np.asarray(adj)[order][:, order].T),
        "num_neighbors": np.ascontiguousarray(L0_gnn_num_neighbors),
        "fc_t": np.ascontiguousarray(np.asarray(L0_gnn_fc_w).T),
        "fc_b": np.ascontiguousarray(L0_gnn_fc_b),
    }
    nc = _bacc.Bacc("TRN2", target_bir_lowering=False, num_devices=1)
    args = [nc.dram_tensor(k, v.shape, mybir.dt.from_np(v.dtype), kind="ExternalInput").ap() for k, v in arrays.items()]
    out = nc.dram_tensor("out", (n, f), F32, kind="ExternalOutput").ap()
    gnn_layer(nc, *args, out)
    r = _run(nc, [arrays], core_ids=[0])
    return r.results[0]["out"]
```

```python
from contextlib import ExitStack

import numpy as np

import concourse.bass as bass
from concourse import mybir

ALU = mybir.AluOpType
ACT = mybir.ActivationFunctionType
F32 = mybir.dt.float32
F32R = mybir.dt.float32r
AX_X = mybir.AxisListType.X

P = 128
BANK = 512
BANK_TILES = BANK // P
RAW = 6
SPLITS = RAW - 1
HALVES = 3
PEEL = (9, 15, 9)
ROUND = 8
LN_EPS = 1e-5
DIV_EPS = 1e-7


def gnn_layer(nc, x, adj_t, num_neighbors, fc_t, fc_b, out):
    N, F = x.shape
    CH = N // P
    REM = N - CH * P
    TILES = CH + 1
    assert 0 < REM <= 32 and TILES % ROUND == 0 and all((CH - k) % RAW == 0 for k in PEEL) and 2 * F == P

    GROUPS = [(0, 16, 0), (16, 16, 4), (32, 8, 2)]
    G = len(GROUPS)
    assert sum(g[1] for g in GROUPS) == TILES
    WIDE = GROUPS[0][1] * P
    ROUNDS = TILES // ROUND
    SUMS_AT = HALVES - 1
    TRANSPOSE_AT = {1 + 2 * r: r for r in range(ROUNDS)}
    HT_AT = {c + HALVES: r for c, r in TRANSPOSE_AT.items()}
    SELF_AT = {c + 2: r for c, r in TRANSPOSE_AT.items()}
    SELF_OUT_AT = {c + HALVES: r for c, r in SELF_AT.items()}
    NEIGHBOR_AT = [{}, {5: 0, 9: 1}, {2: 2, 3: 3}]
    FINISH_AT = [{c + HALVES: r for c, r in k.items()} for k in NEIGHBOR_AT]

    def cols(g):
        t0, tiles, _ = GROUPS[g]
        return t0 * P, min(N, (t0 + tiles) * P) - t0 * P

    def banks(g):
        w = cols(g)[1]
        return [(GROUPS[g][2] + b, b * BANK, min(BANK, w - b * BANK)) for b in range(-(-w // BANK))]

    def split_index(q, s):
        return q * SPLITS + s

    def half_slot(s):
        return s % HALVES

    def half_slot_free(n, s):
        last = [s - d for d in range(1, RAW + 1) if (s - d) % RAW != SPLITS and half_slot((s - d) % RAW) == half_slot(s)][0]
        return n + (last - s) + 1

    with ExitStack() as ctx:
        def sb(name, shape, dt=F32):
            return ctx.enter_context(nc.sbuf_tensor(name, shape, dt))

        def sem(name):
            return ctx.enter_context(nc.semaphore(name))

        raw = [sb(f"raw{s}", [P, WIDE]) for s in range(RAW)]
        hi = [sb(f"hi{s}", [P, WIDE], F32R) for s in range(HALVES)]
        lo = [sb(f"lo{s}", [P, WIDE], F32R) for s in range(HALVES)]
        adj_rem = sb("adj_rem", [REM, WIDE])
        x_sb = sb("x_sb", [P, TILES, F])
        h_sb = sb("h_sb", [P, TILES, F])
        square = sb("square", [P, TILES, F])
        self_sb = sb("self_sb", [P, TILES, F])
        h_parts = sb("h_parts", [P, TILES, 2, F], F32R)
        w_split = [sb(f"w_split{s}", [P, 2 * F], F32R) for s in range(SPLITS)]
        w_plain = sb("w_plain", [P, 2 * F])
        w_rem = sb("w_rem", [REM, 2 * F])
        ht = [sb(f"ht{i}", [F + 1, ROUND * P]) for i in range(2)]
        sums = sb("sums", [P, WIDE])
        prod = sb("prod", [P, ROUND * F])
        w_self = sb("w_self", [F + 1, F])
        w_nbr = sb("w_nbr", [2 * F, F])
        nn = sb("nn", [P, TILES])
        rnn = sb("rnn", [P, TILES])
        ident = sb("ident", [P, P])
        mean = sb("mean", [P, TILES])
        var = sb("var", [P, TILES])
        std = sb("std", [P, TILES])
        rstd = sb("rstd", [P, TILES])

        psum = [ctx.enter_context(nc.psum_tensor(f"bank{b}", [P, BANK], F32)) for b in range(8)]
        T_BANKS, S_BANK, Y_BANK = (2, 3), 0, [1, 1, 0, 1, 0]

        x_cleared = sem("x_cleared")
        x_loaded = [sem("x_loaded_first"), sem("x_loaded_rest")]
        nn_cleared = sem("nn_cleared")
        nn_loaded = sem("nn_loaded")
        weights_loaded = sem("weights_loaded")
        raw_loaded = [sem(f"raw_loaded{s}") for s in range(RAW)]
        rem_loaded = sem("rem_loaded")
        ln_dve = sem("ln_dve")
        ln_act = sem("ln_act")
        ident_cleared = sem("ident_cleared")
        ident_ready = sem("ident_ready")
        ones_ready = sem("ones_ready")
        h_hi_done = sem("h_hi_done")
        h_lo_done = sem("h_lo_done")
        plain_cleared = sem("plain_cleared")
        rem_ready = sem("rem_ready")
        staged = sem("staged")
        hi_done = sem("hi_done")
        lo_done = sem("lo_done")
        pe_done = sem("pe_done")
        rem_done = sem("rem_done")
        ht_transposed = sem("ht_transposed")
        ht_copied = sem("ht_copied")
        self_summed = sem("self_summed")
        self_copied = sem("self_copied")
        sums_copied = sem("sums_copied")
        y_ready = sem("y_ready")
        combine = sem("combine")
        out_ready = sem("out_ready")
        stored = sem("stored")
        rnn_chain = sem("rnn_chain")
        table_loaded = sem("table_loaded")

        LN_OPS = 8
        PARTS = [(0, ROUND), (ROUND, TILES)]

        x_main = x[0:CH * P, :].rearrange("(p t) f -> p t f", t=CH)
        nn_main = num_neighbors[0:CH * P].rearrange("(p t) -> p t", t=CH)
        nn_rem = num_neighbors[CH * P:N].rearrange("(p t) -> p t", t=1)
        out_main = out[0:CH * P, :].rearrange("(p t) f -> p t f", t=CH)
        bias_row = fc_b.rearrange("(a f) -> a f", a=1)

        def bcast(v):
            return v.unsqueeze(2).to_broadcast([P, v.shape[1], F])

        def steps(eng, g, step, between=None):
            for c in range(PEEL[g]):
                n = g * CH + c
                step(c, n, n // RAW, n % RAW)
                if between is not None:
                    between(c)
            with eng.Fori(0, (CH - PEEL[g]) // RAW) as it:
                for j in range(RAW):
                    c0 = PEEL[g] + j
                    n0 = g * CH + c0
                    step(it * RAW + c0, it * RAW + n0, it + n0 // RAW, n0 % RAW)

        def started(n, back):
            return not isinstance(n, int) or n >= back

        block = ctx.enter_context(nc.Block())

        @block.sync
        def _(sp):
            def load(g):
                c0, w = cols(g)

                def step(c, n, q, s):
                    if started(n, RAW):
                        if s < SPLITS:
                            sp.wait_ge(lo_done, split_index(q - 1, s) + 1)
                        else:
                            sp.wait_ge(pe_done, n - RAW + 1)
                    k0 = c * P
                    sp.dma_start(raw[s][:, 0:w], adj_t[bass.ds(k0, P), c0:c0 + w]).then_inc(raw_loaded[s], 16)
                return step

            def load_rem(g):
                c0, w = cols(g)
                if g:
                    sp.wait_ge(rem_done, g)
                sp.dma_start(adj_rem[:, 0:w], adj_t[CH * P:N, c0:c0 + w]).then_inc(rem_loaded, 16)

            def store(t0, t1):
                n_rows = min(t1, CH) - t0
                sp.dma_start(out_main[:, t0:t0 + n_rows, :], self_sb[:, t0:t0 + n_rows, :]).then_inc(stored, 16)

            sp.dma_start(x_sb[:, 0:ROUND, :], x_main[:, 0:ROUND, :]).then_inc(x_loaded[0], 16)
            sp.dma_start(x_sb[:, ROUND:CH, :], x_main[:, ROUND:CH, :]).then_inc(x_loaded[1], 16)
            sp.wait_ge(x_cleared, 1)
            sp.dma_start(x_sb[0:REM, CH, :], x[CH * P:N, :]).then_inc(x_loaded[1], 16)
            for g in range(G):
                steps(sp, g, load(g), lambda c, g=g: load_rem(g) if c == PEEL[g] - 1 else None)
                if g:
                    t0, tiles, _ = GROUPS[g - 1]
                    sp.wait_ge(out_ready, (t0 + tiles) // ROUND)
                    store(t0, t0 + tiles)
            t0, tiles, _ = GROUPS[G - 1]
            sp.wait_ge(out_ready, TILES // ROUND)
            store(t0, t0 + tiles)
            sp.dma_start(out[CH * P:N, :], self_sb[0:REM, CH, :]).then_inc(stored, 16)
            sp.wait_ge(stored, 16 * (G + 1))

        @block.gpsimd
        def _(pool):
            nc.gpsimd.memset(ident[:], 0.0).then_inc(ident_cleared, 1)
            pool.wait_ge(ident_cleared, 1)
            nc.gpsimd.affine_select(out=ident[:], in_=ident[:], compare_op=ALU.not_equal, fill=1.0, base=0,
                                    pattern=[[-1, P]], channel_multiplier=1).then_inc(ident_ready, 1)
            pool.wait_ge(plain_cleared, 2)
            pool.wait_ge(h_hi_done, 1)
            pool.wait_ge(h_lo_done, 1)

            def step(c, n, q, s):
                if started(n, RAW):
                    pool.wait_ge(pe_done, n - RAW + 1)
                if s < SPLITS:
                    nc.gpsimd.tensor_copy(w_split[s][:].rearrange("p (a b f) -> p a b f", a=1, b=2),
                                          h_parts[:, bass.ds(c, 1), :, :]).then_inc(staged, 1)
                else:
                    nc.gpsimd.tensor_copy(w_plain[:, 0:F].rearrange("p (a f) -> p a f", a=1),
                                          h_sb[:, bass.ds(c, 1), :]).then_inc(staged, 1)

            def rest_of_h(c):
                if c == ROUND - 1:
                    pool.wait_ge(h_hi_done, 2)
                    pool.wait_ge(h_lo_done, 2)
                    nc.gpsimd.tensor_copy(w_rem[:, 0:F], h_sb[0:REM, CH, :]).then_inc(rem_ready, 1)

            for g in range(G):
                steps(pool, g, step, rest_of_h if g == 0 else None)

        @block.scalar
        def _(act):
            act.wait_ge(nn_cleared, 1)
            nc.scalar.activation(std[:, 0:1], nn[:, 0:1], ACT.Sqrt).then_inc(table_loaded, 1)
            act.wait_ge(table_loaded, 1)
            act.dma_start(nn[:, 0:CH], nn_main).then_inc(nn_loaded, 16)
            act.dma_start(nn[0:REM, CH:TILES], nn_rem).then_inc(nn_loaded, 16)
            act.dma_start(w_self[0:F, :], fc_t[0:F, :]).then_inc(weights_loaded, 16)
            act.dma_start(w_self[F:F + 1, :], bias_row).then_inc(weights_loaded, 16)
            act.dma_start(w_nbr[0:F, :], fc_t[F:2 * F, :]).then_inc(weights_loaded, 16)
            act.dma_start(w_nbr[F:2 * F, :], fc_t[F:2 * F, :]).then_inc(weights_loaded, 16)

            def high(g):
                w = cols(g)[1]

                def step(c, n, q, s):
                    if s == SPLITS:
                        return
                    act.wait_ge(raw_loaded[s], 16 * q + 16)
                    free = half_slot_free(n, s)
                    if not isinstance(free, int) or free > 0:
                        act.wait_ge(pe_done, free)
                    nc.scalar.activation(hi[half_slot(s)][:, 0:w], raw[s][:, 0:w], ACT.Copy).then_inc(hi_done, 1)
                return step

            def ln_square(part):
                t0, t1 = PARTS[part]
                act.wait_ge(ln_dve, LN_OPS * part + 3)
                nc.scalar.activation(square[:, t0:t1, :], h_sb[:, t0:t1, :], ACT.Square).then_inc(ln_act, 1)

            def ln_std(part):
                t0, t1 = PARTS[part]
                act.wait_ge(ln_dve, LN_OPS * part + 5)
                nc.scalar.activation(std[:, t0:t1], var[:, t0:t1], ACT.Sqrt).then_inc(ln_act, 1)

            def split_h(part):
                t0, t1 = PARTS[part]
                act.wait_ge(ln_dve, LN_OPS * (part + 1))
                nc.scalar.activation(h_parts[:, t0:t1, 0, :], h_sb[:, t0:t1, :], ACT.Copy).then_inc(h_hi_done, 1)

            def copy_ht(r):
                for i, b in enumerate(T_BANKS):
                    act.wait_ge(ht_transposed, 2 * r + i + 1)
                    if r >= 2 and i == 0:
                        act.wait_ge(self_summed, r - 1)
                    nc.scalar.activation(ht[r % 2][0:F, i * BANK:(i + 1) * BANK], psum[b][0:F, :],
                                         ACT.Copy).then_inc(ht_copied, 1)

            def copy_sums(g):
                act.wait_ge(rem_done, g + 1)
                if g:
                    act.wait_ge(y_ready, (GROUPS[g - 1][0] + GROUPS[g - 1][1]) // ROUND)
                for b, c0, w in banks(g):
                    nc.scalar.activation(sums[:, c0:c0 + w], psum[b][:, 0:w], ACT.Copy).then_inc(sums_copied, 1)

            ln_square(0)
            ln_std(0)
            split_h(0)
            for g in range(G):
                def between(c, g=g):
                    if g == 0 and 1 <= c <= 3:
                        (ln_square, ln_std, split_h)[c - 1](1)
                    if g and c == SUMS_AT:
                        copy_sums(g - 1)
                    if g == 1 and c in HT_AT:
                        copy_ht(HT_AT[c])
                steps(act, g, high(g), between)
            copy_sums(G - 1)

        @block.vector
        def _(dve):
            nc.vector.memset(x_sb[:, CH, :], 0.0).then_inc(x_cleared, 1)
            nc.vector.memset(nn[:], 1.0).then_inc(nn_cleared, 1)
            for i in range(2):
                nc.vector.memset(ht[i][F:F + 1, :], 1.0).then_inc(ones_ready, 1)
            nc.vector.memset(w_plain[:], 0.0).then_inc(plain_cleared, 1)
            nc.vector.memset(w_rem[:], 0.0).then_inc(plain_cleared, 1)
            def low(g):
                w = cols(g)[1]

                def step(c, n, q, s):
                    if s == SPLITS:
                        return
                    dve.wait_ge(hi_done, split_index(q, s) + 1)
                    i = half_slot(s)
                    nc.vector.tensor_tensor(lo[i][:, 0:w], raw[s][:, 0:w], hi[i][:, 0:w].bitcast(F32),
                                            ALU.subtract).then_inc(lo_done, 1)
                return step

            def invert_neighbors():
                dve.wait_ge(nn_loaded, 32)
                nc.vector.tensor_scalar(nn[:], nn[:], DIV_EPS, None, ALU.add).then_inc(rnn_chain, 1)
                dve.wait_ge(rnn_chain, 1)
                nc.vector.reciprocal(rnn[:], nn[:]).then_inc(rnn_chain, 1)

            def center(part):
                t0, t1 = PARTS[part]
                if part:
                    dve.wait_ge(x_loaded[1], 32)
                else:
                    dve.wait_ge(x_loaded[0], 16)
                nc.vector.tensor_reduce(mean[:, t0:t1], x_sb[:, t0:t1, :], AX_X, ALU.add).then_inc(ln_dve, 1)
                dve.wait_ge(ln_dve, LN_OPS * part + 1)
                nc.vector.tensor_scalar(mean[:, t0:t1], mean[:, t0:t1], 1.0 / F, None, ALU.mult).then_inc(ln_dve, 1)
                dve.wait_ge(ln_dve, LN_OPS * part + 2)
                nc.vector.tensor_tensor(h_sb[:, t0:t1, :], x_sb[:, t0:t1, :], bcast(mean[:, t0:t1]),
                                        ALU.subtract).then_inc(ln_dve, 1)

            def variance(part):
                t0, t1 = PARTS[part]
                dve.wait_ge(ln_act, 2 * part + 1)
                nc.vector.tensor_reduce(var[:, t0:t1], square[:, t0:t1, :], AX_X, ALU.add).then_inc(ln_dve, 1)
                dve.wait_ge(ln_dve, LN_OPS * part + 4)
                nc.vector.tensor_scalar(var[:, t0:t1], var[:, t0:t1], 1.0 / F, LN_EPS, ALU.mult,
                                        ALU.add).then_inc(ln_dve, 1)

            def normalize(part):
                t0, t1 = PARTS[part]
                dve.wait_ge(ln_act, 2 * part + 2)
                nc.vector.reciprocal(rstd[:, t0:t1], std[:, t0:t1]).then_inc(ln_dve, 1)
                dve.wait_ge(ln_dve, LN_OPS * part + 6)
                nc.vector.tensor_tensor(h_sb[:, t0:t1, :], h_sb[:, t0:t1, :], bcast(rstd[:, t0:t1]),
                                        ALU.mult).then_inc(ln_dve, 1)
                dve.wait_ge(ln_dve, LN_OPS * part + 7)
                nc.vector.tensor_scalar(h_sb[:, t0:t1, :], h_sb[:, t0:t1, :], 0.0, None, ALU.max).then_inc(ln_dve, 1)

            def low_h(part):
                t0, t1 = PARTS[part]
                dve.wait_ge(h_hi_done, part + 1)
                nc.vector.tensor_tensor(h_parts[:, t0:t1, 1, :], h_sb[:, t0:t1, :],
                                        h_parts[:, t0:t1, 0, :].bitcast(F32), ALU.subtract).then_inc(h_lo_done, 1)

            def copy_self(r):
                dve.wait_ge(self_summed, r + 1)
                nc.vector.tensor_copy(self_sb[:, r * ROUND:(r + 1) * ROUND, :],
                                      psum[S_BANK][:].rearrange("p (t f) -> p t f", f=F)).then_inc(self_copied, 1)

            def finish(r):
                t = slice(r * ROUND, (r + 1) * ROUND)
                p3 = prod[:].rearrange("p (t f) -> p t f", f=F)
                dve.wait_ge(y_ready, r + 1)
                if r == 0:
                    dve.wait_ge(rnn_chain, 2)
                nc.vector.tensor_tensor(p3, psum[Y_BANK[r]][:].rearrange("p (t f) -> p t f", f=F),
                                        bcast(rnn[:, t]), ALU.mult).then_inc(combine, 1)
                dve.wait_ge(combine, 2 * r + 1)
                dve.wait_ge(self_copied, r + 1)
                nc.vector.tensor_tensor(self_sb[:, t, :], p3, self_sb[:, t, :], ALU.add).then_inc(combine, 1)
                dve.wait_ge(combine, 2 * r + 2)
                nc.vector.scalar_tensor_tensor(self_sb[:, t, :], self_sb[:, t, :], 0.0, x_sb[:, t, :],
                                               ALU.max, ALU.add).then_inc(out_ready, 1)

            center(0)
            variance(0)
            normalize(0)
            low_h(0)
            for g in range(G):
                def between(c, g=g):
                    if g == 0 and c <= 3:
                        (center, variance, normalize, low_h)[c](1)
                    if g == 0 and c == PEEL[g] - 1:
                        invert_neighbors()
                    if g == 1 and c in SELF_OUT_AT:
                        copy_self(SELF_OUT_AT[c])
                    if c in FINISH_AT[g]:
                        finish(FINISH_AT[g][c])
                steps(dve, g, low(g), between)
            finish(GROUPS[G - 1][0] // ROUND)

        @block.tensor
        def _(pe):
            def transpose_h(r):
                if r:
                    pe.wait_ge(ht_copied, 2 * r)
                else:
                    pe.wait_ge(sums_copied, len(banks(0)))
                for i in range(ROUND):
                    t = r * ROUND + i
                    b = T_BANKS[i // BANK_TILES]
                    last = nc.tensor.transpose(psum[b][0:F, (i % BANK_TILES) * P:(i % BANK_TILES + 1) * P],
                                               h_sb[:, t, :], ident[:])
                    if i % BANK_TILES == BANK_TILES - 1:
                        last.then_inc(ht_transposed, 1)

            def self_part(r):
                pe.wait_ge(ht_copied, 2 * (r + 1))
                if r:
                    pe.wait_ge(self_copied, r)
                for i in range(ROUND):
                    last = nc.tensor.matmul(psum[S_BANK][:, i * F:(i + 1) * F],
                                            ht[r % 2][:, i * P:(i + 1) * P], w_self[:], start=True, stop=True)
                last.then_inc(self_summed, 1)

            def neighbor_part(r, g):
                i0 = r * ROUND - GROUPS[g][0]
                before = sum(len(banks(k)) for k in range(g))
                pe.wait_ge(sums_copied, before + min(len(banks(g)), -(-(i0 + ROUND) // BANK_TILES)))
                users = [k for k in range(r) if Y_BANK[k] == Y_BANK[r]]
                if users:
                    pe.wait_ge(combine, 2 * users[-1] + 1)
                for i in range(ROUND):
                    last = nc.tensor.matmul(psum[Y_BANK[r]][:, i * F:(i + 1) * F],
                                            sums[:, (i0 + i) * P:(i0 + i + 1) * P], w_nbr[:], start=True, stop=True)
                last.then_inc(y_ready, 1)

            def remainder(g):
                pe.wait_ge(rem_loaded, 16 * (g + 1))
                for b, c0, w in banks(g):
                    last = nc.tensor.matmul(psum[b][:, 0:w], w_rem[:], adj_rem[:, c0:c0 + w], start=False, stop=True)
                last.then_inc(rem_done, 1)

            def multiply(g):
                def step(c, n, q, s):
                    first = isinstance(c, int) and c == 0
                    pe.wait_ge(staged, n + 1)
                    if s < SPLITS:
                        i = half_slot(s)
                        pe.wait_ge(hi_done, split_index(q, s) + 1)
                        for b, c0, w in banks(g):
                            nc.tensor.matmul(psum[b][:, 0:w], w_split[s][:], hi[i][:, c0:c0 + w],
                                             start=first, stop=False)
                        pe.wait_ge(lo_done, split_index(q, s) + 1)
                        for b, c0, w in banks(g):
                            last = nc.tensor.matmul(psum[b][:, 0:w], w_split[s][:], lo[i][:, c0:c0 + w],
                                                    start=False, stop=False)
                    else:
                        pe.wait_ge(raw_loaded[s], 16 * q + 16)
                        for b, c0, w in banks(g):
                            last = nc.tensor.matmul(psum[b][:, 0:w], w_plain[:], raw[s][:, c0:c0 + w],
                                                    start=first, stop=False)
                    last.then_inc(pe_done, 1)
                return step

            for g in range(G):
                if g == 2:
                    pe.wait_ge(ht_copied, 2 * (TILES // ROUND))

                def between(c, g=g):
                    if g == 1 and c in SELF_AT:
                        self_part(SELF_AT[c])
                    if g == 1 and c in TRANSPOSE_AT:
                        transpose_h(TRANSPOSE_AT[c])
                    if c in NEIGHBOR_AT[g]:
                        neighbor_part(NEIGHBOR_AT[g][c], g - 1)
                steps(pe, g, multiply(g), between)
                if g == 0:
                    pe.wait_ge(rem_ready, 1)
                    pe.wait_ge(ident_ready, 1)
                    pe.wait_ge(ones_ready, 2)
                    pe.wait_ge(weights_loaded, 64)
                remainder(g)
            neighbor_part(GROUPS[G - 1][0] // ROUND, G - 1)


def kernel(x, adj, L0_gnn_num_neighbors, L0_gnn_fc_w, L0_gnn_fc_b):
    import concourse.bacc as _bacc
    from concourse.bass_utils import run_bass_kernel_spmd as _run

    x = np.ascontiguousarray(x)
    n, f = x.shape
    whole = n // P * P
    order = np.concatenate([np.arange(whole).reshape(P, whole // P).T.ravel(), np.arange(whole, n)])
    arrays = {
        "x": x,
        "adj_t": np.ascontiguousarray(np.asarray(adj)[order][:, order].T),
        "num_neighbors": np.ascontiguousarray(L0_gnn_num_neighbors),
        "fc_t": np.ascontiguousarray(np.asarray(L0_gnn_fc_w).T),
        "fc_b": np.ascontiguousarray(L0_gnn_fc_b),
    }
    nc = _bacc.Bacc("TRN2", target_bir_lowering=False, num_devices=1)
    args = [nc.dram_tensor(k, v.shape, mybir.dt.from_np(v.dtype), kind="ExternalInput").ap() for k, v in arrays.items()]
    out = nc.dram_tensor("out", (n, f), F32, kind="ExternalOutput").ap()
    gnn_layer(nc, *args, out)
    r = _run(nc, [arrays], core_ids=[0])
    return r.results[0]["out"]
```

```python
from contextlib import ExitStack

import numpy as np

import concourse.bass as bass
from concourse import mybir

ALU = mybir.AluOpType
ACT = mybir.ActivationFunctionType
F32 = mybir.dt.float32
F32R = mybir.dt.float32r
AX_X = mybir.AxisListType.X

P = 128
BANK = 512
BANK_TILES = BANK // P
RAW = 7
PLAIN = 4
SPLITS = RAW - 1
EXTRA = 3
HALVES = 3
PEEL = (10, 24, 10)
LAST = 1
ROUND = 8
LN_EPS = 1e-5
DIV_EPS = 1e-7


GROUPS = [(0, 16, 0), (16, 16, 4), (32, 8, 2)]
ALIGN = 64


def gnn_layer(nc, x, adj_groups, num_neighbors, fc_t, fc_b, out):
    N, F = x.shape
    CH = N // P
    REM = N - CH * P
    TILES = CH + 1
    assert 0 < REM <= 32 and TILES % ROUND == 0 and all((CH - k - LAST) % RAW == 0 for k in PEEL) and 2 * F == P

    G = len(GROUPS)
    assert sum(g[1] for g in GROUPS) == TILES
    WIDE = GROUPS[0][1] * P
    ROUNDS = TILES // ROUND
    REM_AT = 7
    SUMS_AT = HALVES - 1
    TRANSPOSE_AT = {1 + 3 * r: r for r in range(ROUNDS)}
    HT_AT = {c + HALVES: r for c, r in TRANSPOSE_AT.items()}
    SELF_AT = {c + 2: r for c, r in TRANSPOSE_AT.items()}
    SELF_OUT_AT = {c + HALVES: r for c, r in SELF_AT.items()}
    NEIGHBOR_AT = [{}, {5: 0, 14: 1}, {2: 2, 5: 3}]
    FINISH_AT = [{c + HALVES: r for c, r in k.items()} for k in NEIGHBOR_AT]

    def cols(g):
        t0, tiles, _ = GROUPS[g]
        return t0 * P, min(N, (t0 + tiles) * P) - t0 * P

    def banks(g):
        w = cols(g)[1]
        return [(GROUPS[g][2] + b, b * BANK, min(BANK, w - b * BANK)) for b in range(-(-w // BANK))]

    def plain(n, s):
        return s == PLAIN or (isinstance(n, int) and n < EXTRA)

    def split_index(q, s):
        return q * SPLITS + s - (s > PLAIN) - EXTRA

    def half_slot(s):
        return (s - (s > PLAIN)) % HALVES

    def half_slot_free(n, s):
        last = [s - d for d in range(1, RAW + 1) if (s - d) % RAW != PLAIN and half_slot((s - d) % RAW) == half_slot(s)][0]
        return n + (last - s) + 1

    with ExitStack() as ctx:
        def sb(name, shape, dt=F32):
            return ctx.enter_context(nc.sbuf_tensor(name, shape, dt))

        def sem(name):
            return ctx.enter_context(nc.semaphore(name))

        raw = [sb(f"raw{s}", [P, WIDE]) for s in range(RAW)]
        hi = [sb(f"hi{s}", [P, WIDE], F32R) for s in range(HALVES)]
        lo = [sb(f"lo{s}", [P, WIDE], F32R) for s in range(HALVES)]
        adj_rem = sb("adj_rem", [REM, WIDE])
        x_sb = sb("x_sb", [P, TILES, F])
        h_sb = sb("h_sb", [P, TILES, F])
        square = sb("square", [P, TILES, F])
        self_sb = sb("self_sb", [P, TILES, F])
        h_parts = sb("h_parts", [P, TILES, 2, F], F32R)
        w_split = [sb(f"w_split{s}", [P, 2 * F], F32R) for s in range(RAW)]
        w_plain = {s: sb(f"w_plain{s}", [P, 2 * F]) for s in (*range(EXTRA), PLAIN)}
        w_rem = sb("w_rem", [REM, 2 * F])
        ht = [sb(f"ht{i}", [F + 1, ROUND * P]) for i in range(2)]
        sums = sb("sums", [P, WIDE])
        prod = sb("prod", [P, ROUND * F])
        w_self = sb("w_self", [F + 1, F])
        w_nbr = sb("w_nbr", [2 * F, F])
        nn = sb("nn", [P, TILES])
        rnn = sb("rnn", [P, TILES])
        ident = sb("ident", [P, P])
        mean = sb("mean", [P, TILES])
        var = sb("var", [P, TILES])
        std = sb("std", [P, TILES])
        rstd = sb("rstd", [P, TILES])

        psum = [ctx.enter_context(nc.psum_tensor(f"bank{b}", [P, BANK], F32)) for b in range(8)]
        T_BANKS, S_BANK = (2, 3), 0
        PIECES = [(0, 8, 1), (8, 16, 1), (16, 24, 0), (24, 32, 1), (32, 36, 0), (36, 40, 1)]
        END = 4
        assert (G * CH - 1) % RAW == PLAIN

        x_cleared = sem("x_cleared")
        x_loaded = [sem("x_loaded_first"), sem("x_loaded_rest")]
        nn_cleared = sem("nn_cleared")
        nn_loaded = sem("nn_loaded")
        weights_loaded = sem("weights_loaded")
        raw_loaded = [sem(f"raw_loaded{s}") for s in range(RAW)]
        rem_loaded = sem("rem_loaded")
        ln_dve = sem("ln_dve")
        ln_act = sem("ln_act")
        ident_cleared = sem("ident_cleared")
        ident_ready = sem("ident_ready")
        ones_ready = sem("ones_ready")
        h_hi_done = sem("h_hi_done")
        h_lo_done = sem("h_lo_done")
        plain_cleared = sem("plain_cleared")
        rem_ready = sem("rem_ready")
        staged = sem("staged")
        hi_done = sem("hi_done")
        lo_done = sem("lo_done")
        pe_done = sem("pe_done")
        rem_done = sem("rem_done")
        ht_transposed = sem("ht_transposed")
        ht_copied = sem("ht_copied")
        self_summed = sem("self_summed")
        self_copied = sem("self_copied")
        sums_copied = sem("sums_copied")
        y_ready = sem("y_ready")
        combine = sem("combine")
        bank_done = sem("bank_done")
        last_sums_copied = sem("last_sums_copied")
        rem_stored = sem("rem_stored")
        out_ready = sem("out_ready")
        stored = sem("stored")
        rnn_chain = sem("rnn_chain")
        table_loaded = sem("table_loaded")

        LN_OPS = 8
        PARTS = [(0, ROUND), (ROUND, TILES)]

        x_main = x[0:CH * P, :].rearrange("(p t) f -> p t f", t=CH)
        nn_main = num_neighbors[0:CH * P].rearrange("(p t) -> p t", t=CH)
        nn_rem = num_neighbors[CH * P:N].rearrange("(p t) -> p t", t=1)
        out_main = out[0:CH * P, :].rearrange("(p t) f -> p t f", t=CH)
        bias_row = fc_b.rearrange("(a f) -> a f", a=1)

        def bcast(v):
            return v.unsqueeze(2).to_broadcast([P, v.shape[1], F])

        def steps(eng, g, step, between=None):
            def written_out(c):
                n = g * CH + c
                step(c, n, n // RAW, n % RAW)

            for c in range(PEEL[g]):
                written_out(c)
                if between is not None:
                    between(c)
            with eng.Fori(0, (CH - PEEL[g] - LAST) // RAW) as it:
                for j in range(RAW):
                    c0 = PEEL[g] + j
                    n0 = g * CH + c0
                    step(it * RAW + c0, it * RAW + n0, it + n0 // RAW, n0 % RAW)
            for c in range(CH - LAST, CH):
                written_out(c)

        def started(n, back):
            return not isinstance(n, int) or n >= back

        block = ctx.enter_context(nc.Block())

        @block.sync
        def _(sp):
            def load(g):
                w = cols(g)[1]

                def step(c, n, q, s):
                    if started(n, RAW):
                        if not plain(n - RAW, s):
                            sp.wait_ge(lo_done, split_index(q - 1, s) + 1)
                        else:
                            sp.wait_ge(pe_done, n - RAW + 1)
                    k0 = c * P
                    sp.dma_start(raw[s][:, 0:w], adj_groups[g][bass.ds(k0, P), 0:w]).then_inc(raw_loaded[s], 16)
                return step

            def load_rem(g):
                w = cols(g)[1]
                if g:
                    sp.wait_ge(rem_done, g)
                sp.dma_start(adj_rem[:, 0:w], adj_groups[g][CH * P:N, 0:w]).then_inc(rem_loaded, 16)

            def store(t0, t1):
                n_rows = min(t1, CH) - t0
                sp.dma_start(out_main[:, t0:t0 + n_rows, :], self_sb[:, t0:t0 + n_rows, :]).then_inc(stored, 16)

            sp.dma_start(x_sb[:, 0:ROUND, :], x_main[:, 0:ROUND, :]).then_inc(x_loaded[0], 16)
            sp.dma_start(x_sb[:, ROUND:CH, :], x_main[:, ROUND:CH, :]).then_inc(x_loaded[1], 16)
            sp.wait_ge(x_cleared, 1)
            sp.dma_start(x_sb[0:REM, CH, :], x[CH * P:N, :]).then_inc(x_loaded[1], 16)
            def between(g):
                def other(c):
                    if c == REM_AT - 2:
                        load_rem(g)
                    if g == 0 and c == RAW - 1:
                        load_small()
                return other

            def load_small():
                sp.wait_ge(table_loaded, 1)
                sp.dma_start(nn[:, 0:CH], nn_main).then_inc(nn_loaded, 16)
                sp.dma_start(nn[0:REM, CH:TILES], nn_rem).then_inc(nn_loaded, 16)
                sp.dma_start(w_self[0:F, :], fc_t[0:F, :]).then_inc(weights_loaded, 16)
                sp.dma_start(w_self[F:F + 1, :], bias_row).then_inc(weights_loaded, 16)
                sp.dma_start(w_nbr[0:F, :], fc_t[F:2 * F, :]).then_inc(weights_loaded, 16)
                sp.dma_start(w_nbr[F:2 * F, :], fc_t[F:2 * F, :]).then_inc(weights_loaded, 16)

            for g in range(G):
                steps(sp, g, load(g), between(g))
                if g:
                    t0, tiles, _ = GROUPS[g - 1]
                    sp.wait_ge(out_ready, 2 * g)
                    store(t0, t0 + tiles)
            for k in range(END, len(PIECES)):
                sp.wait_ge(out_ready, k + 1)
                store(PIECES[k][0], PIECES[k][1])
            sp.wait_ge(stored, 16 * (G - 1 + len(PIECES) - END))

        @block.gpsimd
        def _(pool):
            nc.gpsimd.memset(ident[:], 0.0).then_inc(ident_cleared, 1)
            pool.wait_ge(ident_cleared, 1)
            nc.gpsimd.affine_select(out=ident[:], in_=ident[:], compare_op=ALU.not_equal, fill=1.0, base=0,
                                    pattern=[[-1, P]], channel_multiplier=1).then_inc(ident_ready, 1)
            pool.wait_ge(plain_cleared, len(w_plain) + 1)
            pool.wait_ge(h_hi_done, 1)
            pool.wait_ge(h_lo_done, 1)

            def step(c, n, q, s):
                if started(n, RAW):
                    pool.wait_ge(pe_done, n - RAW + 1)
                if not plain(n, s):
                    nc.gpsimd.tensor_copy(w_split[s][:].rearrange("p (a b f) -> p a b f", a=1, b=2),
                                          h_parts[:, bass.ds(c, 1), :, :]).then_inc(staged, 1)
                else:
                    nc.gpsimd.tensor_copy(w_plain[s][:, 0:F].rearrange("p (a f) -> p a f", a=1),
                                          h_sb[:, bass.ds(c, 1), :]).then_inc(staged, 1)

            def rest_of_h(c):
                if c == ROUND - 1:
                    pool.wait_ge(h_hi_done, 2)
                    pool.wait_ge(h_lo_done, 2)
                    nc.gpsimd.tensor_copy(w_rem[:, 0:F], h_sb[0:REM, CH, :]).then_inc(rem_ready, 1)

            for g in range(G):
                steps(pool, g, step, rest_of_h if g == 0 else None)

        @block.scalar
        def _(act):
            act.wait_ge(nn_cleared, 1)
            nc.scalar.activation(std[:, 0:1], nn[:, 0:1], ACT.Sqrt).then_inc(table_loaded, 1)
            def high(g):
                w = cols(g)[1]

                def step(c, n, q, s):
                    if plain(n, s):
                        return
                    act.wait_ge(raw_loaded[s], 16 * q + 16)
                    free = half_slot_free(n, s)
                    if not isinstance(free, int) or free > 0:
                        act.wait_ge(pe_done, free)
                    nc.scalar.activation(hi[half_slot(s)][:, 0:w], raw[s][:, 0:w], ACT.Copy).then_inc(hi_done, 1)
                return step

            def ln_square(part):
                t0, t1 = PARTS[part]
                act.wait_ge(ln_dve, LN_OPS * part + 3)
                nc.scalar.activation(square[:, t0:t1, :], h_sb[:, t0:t1, :], ACT.Square).then_inc(ln_act, 1)

            def ln_std(part):
                t0, t1 = PARTS[part]
                act.wait_ge(ln_dve, LN_OPS * part + 5)
                nc.scalar.activation(std[:, t0:t1], var[:, t0:t1], ACT.Sqrt).then_inc(ln_act, 1)

            def split_h(part):
                t0, t1 = PARTS[part]
                act.wait_ge(ln_dve, LN_OPS * (part + 1))
                nc.scalar.activation(h_parts[:, t0:t1, 0, :], h_sb[:, t0:t1, :], ACT.Copy).then_inc(h_hi_done, 1)

            def copy_ht(r):
                for i, b in enumerate(T_BANKS):
                    act.wait_ge(ht_transposed, 2 * r + i + 1)
                    if r >= 2 and i == 0:
                        act.wait_ge(self_summed, r - 1)
                    nc.scalar.activation(ht[r % 2][0:F, i * BANK:(i + 1) * BANK], psum[b][0:F, :],
                                         ACT.Copy).then_inc(ht_copied, 1)

            def copy_sums(g):
                if g:
                    act.wait_ge(y_ready, 2 * g)
                if g < G - 1:
                    act.wait_ge(pe_done, CH * (g + 1))
                else:
                    act.wait_ge(bank_done, 1)
                for b, c0, w in banks(g)[:1 if g == G - 1 else None]:
                    nc.scalar.activation(sums[:, c0:c0 + w], psum[b][:, 0:w], ACT.Copy).then_inc(sums_copied, 1)

            ln_square(0)
            ln_std(0)
            split_h(0)
            ln_square(1)
            for g in range(G):
                def between(c, g=g):
                    if g == 0 and c in (3, 5):
                        (ln_std, split_h)[c // 5](1)
                    if g and c == SUMS_AT:
                        copy_sums(g - 1)
                    if g == 1 and c in HT_AT:
                        copy_ht(HT_AT[c])
                steps(act, g, high(g), between)
            copy_sums(G - 1)
            act.wait_ge(out_ready, len(PIECES))
            act.dma_start(out[CH * P:N, :], self_sb[0:REM, CH, :]).then_inc(rem_stored, 16)
            act.wait_ge(rem_stored, 16)

        @block.vector
        def _(dve):
            nc.vector.memset(x_sb[:, CH, :], 0.0).then_inc(x_cleared, 1)
            nc.vector.memset(nn[:], 1.0).then_inc(nn_cleared, 1)
            for i in range(2):
                nc.vector.memset(ht[i][F:F + 1, :], 1.0).then_inc(ones_ready, 1)
            for w in (*w_plain.values(), w_rem):
                nc.vector.memset(w[:], 0.0).then_inc(plain_cleared, 1)
            def low(g):
                w = cols(g)[1]

                def step(c, n, q, s):
                    if plain(n, s):
                        return
                    dve.wait_ge(hi_done, split_index(q, s) + 1)
                    i = half_slot(s)
                    nc.vector.tensor_tensor(lo[i][:, 0:w], raw[s][:, 0:w], hi[i][:, 0:w].bitcast(F32),
                                            ALU.subtract).then_inc(lo_done, 1)
                return step

            def invert_neighbors():
                dve.wait_ge(nn_loaded, 32)
                nc.vector.tensor_scalar(nn[:], nn[:], DIV_EPS, None, ALU.add).then_inc(rnn_chain, 1)
                dve.wait_ge(rnn_chain, 1)
                nc.vector.reciprocal(rnn[:], nn[:]).then_inc(rnn_chain, 1)

            def center(part):
                t0, t1 = PARTS[part]
                if part:
                    dve.wait_ge(x_loaded[1], 32)
                else:
                    dve.wait_ge(x_loaded[0], 16)
                nc.vector.tensor_reduce(mean[:, t0:t1], x_sb[:, t0:t1, :], AX_X, ALU.add).then_inc(ln_dve, 1)
                dve.wait_ge(ln_dve, LN_OPS * part + 1)
                nc.vector.tensor_scalar(mean[:, t0:t1], mean[:, t0:t1], 1.0 / F, None, ALU.mult).then_inc(ln_dve, 1)
                dve.wait_ge(ln_dve, LN_OPS * part + 2)
                nc.vector.tensor_tensor(h_sb[:, t0:t1, :], x_sb[:, t0:t1, :], bcast(mean[:, t0:t1]),
                                        ALU.subtract).then_inc(ln_dve, 1)

            def variance(part):
                t0, t1 = PARTS[part]
                dve.wait_ge(ln_act, 2 * part + 1)
                nc.vector.tensor_reduce(var[:, t0:t1], square[:, t0:t1, :], AX_X, ALU.add).then_inc(ln_dve, 1)
                dve.wait_ge(ln_dve, LN_OPS * part + 4)
                nc.vector.tensor_scalar(var[:, t0:t1], var[:, t0:t1], 1.0 / F, LN_EPS, ALU.mult,
                                        ALU.add).then_inc(ln_dve, 1)

            def normalize(part):
                t0, t1 = PARTS[part]
                dve.wait_ge(ln_act, 2 * part + 2)
                nc.vector.reciprocal(rstd[:, t0:t1], std[:, t0:t1]).then_inc(ln_dve, 1)
                dve.wait_ge(ln_dve, LN_OPS * part + 6)
                nc.vector.tensor_tensor(h_sb[:, t0:t1, :], h_sb[:, t0:t1, :], bcast(rstd[:, t0:t1]),
                                        ALU.mult).then_inc(ln_dve, 1)
                dve.wait_ge(ln_dve, LN_OPS * part + 7)
                nc.vector.tensor_scalar(h_sb[:, t0:t1, :], h_sb[:, t0:t1, :], 0.0, None, ALU.max).then_inc(ln_dve, 1)

            def low_h(part):
                t0, t1 = PARTS[part]
                dve.wait_ge(h_hi_done, part + 1)
                nc.vector.tensor_tensor(h_parts[:, t0:t1, 1, :], h_sb[:, t0:t1, :],
                                        h_parts[:, t0:t1, 0, :].bitcast(F32), ALU.subtract).then_inc(h_lo_done, 1)

            def copy_self(r):
                dve.wait_ge(self_summed, r + 1)
                nc.vector.tensor_copy(self_sb[:, r * ROUND:(r + 1) * ROUND, :],
                                      psum[S_BANK][:].rearrange("p (t f) -> p t f", f=F)).then_inc(self_copied, 1)

            def finish(k):
                t0, t1, b = PIECES[k]
                t = slice(t0, t1)
                p3 = prod[:, 0:(t1 - t0) * F].rearrange("p (t f) -> p t f", f=F)
                dve.wait_ge(y_ready, k + 1)
                if k == 0:
                    dve.wait_ge(rnn_chain, 2)
                nc.vector.tensor_tensor(p3, psum[b][:, 0:(t1 - t0) * F].rearrange("p (t f) -> p t f", f=F),
                                        bcast(rnn[:, t]), ALU.mult).then_inc(combine, 1)
                dve.wait_ge(combine, 2 * k + 1)
                dve.wait_ge(self_copied, -(-t1 // ROUND))
                nc.vector.tensor_tensor(self_sb[:, t, :], p3, self_sb[:, t, :], ALU.add).then_inc(combine, 1)
                dve.wait_ge(combine, 2 * k + 2)
                nc.vector.scalar_tensor_tensor(self_sb[:, t, :], self_sb[:, t, :], 0.0, x_sb[:, t, :],
                                               ALU.max, ALU.add).then_inc(out_ready, 1)

            def copy_last_sums():
                b, c0, w = banks(G - 1)[1]
                dve.wait_ge(y_ready, END)
                dve.wait_ge(bank_done, 2)
                nc.vector.tensor_copy(sums[:, c0:c0 + w], psum[b][:, 0:w]).then_inc(last_sums_copied, 1)

            center(0)
            variance(0)
            normalize(0)
            low_h(0)
            center(1)
            variance(1)
            for g in range(G):
                def between(c, g=g):
                    if g == 0 and c in (3, 5):
                        (normalize, low_h)[c // 5](1)
                    if g == 0 and c == PEEL[g] - 1:
                        invert_neighbors()
                    if g == 1 and c in SELF_OUT_AT:
                        copy_self(SELF_OUT_AT[c])
                    if c in FINISH_AT[g]:
                        finish(FINISH_AT[g][c])
                steps(dve, g, low(g), between)
            copy_last_sums()
            for k in range(END, len(PIECES)):
                finish(k)

        @block.tensor
        def _(pe):
            def transpose_h(r):
                if r:
                    pe.wait_ge(ht_copied, 2 * r)
                else:
                    pe.wait_ge(sums_copied, len(banks(0)))
                for i in range(ROUND):
                    t = r * ROUND + i
                    b = T_BANKS[i // BANK_TILES]
                    last = nc.tensor.transpose(psum[b][0:F, (i % BANK_TILES) * P:(i % BANK_TILES + 1) * P],
                                               h_sb[:, t, :], ident[:])
                    if i % BANK_TILES == BANK_TILES - 1:
                        last.then_inc(ht_transposed, 1)

            def self_part(r):
                pe.wait_ge(ht_copied, 2 * (r + 1))
                if r:
                    pe.wait_ge(self_copied, r)
                for i in range(ROUND):
                    last = nc.tensor.matmul(psum[S_BANK][:, i * F:(i + 1) * F],
                                            ht[r % 2][:, i * P:(i + 1) * P], w_self[:], start=True, stop=True)
                last.then_inc(self_summed, 1)

            def neighbor_part(k):
                t0, t1, b = PIECES[k]
                g = [t0 >= first for first, _, _ in GROUPS].count(True) - 1
                i0 = t0 - GROUPS[g][0]
                if k == len(PIECES) - 1:
                    pe.wait_ge(last_sums_copied, 1)
                else:
                    before = sum(len(banks(j)) for j in range(g))
                    pe.wait_ge(sums_copied, before + (i0 + t1 - t0) // BANK_TILES)
                users = [j for j in range(k) if PIECES[j][2] == b]
                if users:
                    pe.wait_ge(combine, 2 * users[-1] + 1)
                for i in range(t1 - t0):
                    last = nc.tensor.matmul(psum[b][:, i * F:(i + 1) * F],
                                            sums[:, (i0 + i) * P:(i0 + i + 1) * P], w_nbr[:], start=True, stop=True)
                last.then_inc(y_ready, 1)

            def remainder(g):
                pe.wait_ge(rem_ready, 1)
                pe.wait_ge(rem_loaded, 16 * (g + 1))
                for b, c0, w in banks(g):
                    last = nc.tensor.matmul(psum[b][:, 0:w], w_rem[:], adj_rem[:, c0:c0 + w], start=False, stop=False)
                last.then_inc(rem_done, 1)

            def multiply(g):
                def step(c, n, q, s):
                    first = isinstance(c, int) and c == 0
                    end = isinstance(c, int) and c == CH - 1
                    pe.wait_ge(staged, n + 1)
                    if not plain(n, s):
                        i = half_slot(s)
                        pe.wait_ge(hi_done, split_index(q, s) + 1)
                        for b, c0, w in banks(g):
                            nc.tensor.matmul(psum[b][:, 0:w], w_split[s][:], hi[i][:, c0:c0 + w],
                                             start=first, stop=False)
                        pe.wait_ge(lo_done, split_index(q, s) + 1)
                        for b, c0, w in banks(g):
                            last = nc.tensor.matmul(psum[b][:, 0:w], w_split[s][:], lo[i][:, c0:c0 + w],
                                                    start=False, stop=end)
                    else:
                        pe.wait_ge(raw_loaded[s], 16 * q + 16)
                        for b, c0, w in banks(g):
                            last = nc.tensor.matmul(psum[b][:, 0:w], w_plain[s][:], raw[s][:, c0:c0 + w],
                                                    start=first, stop=end)
                            if end and g == G - 1:
                                last.then_inc(bank_done, 1)
                    if not (end and g == G - 1):
                        last.then_inc(pe_done, 1)
                return step

            for g in range(G):
                if g == 2:
                    pe.wait_ge(ht_copied, 2 * (TILES // ROUND))

                def between(c, g=g):
                    if c == REM_AT:
                        remainder(g)
                    if g == 1 and c in SELF_AT:
                        self_part(SELF_AT[c])
                    if g == 1 and c in TRANSPOSE_AT:
                        transpose_h(TRANSPOSE_AT[c])
                    if c in NEIGHBOR_AT[g]:
                        neighbor_part(NEIGHBOR_AT[g][c])
                steps(pe, g, multiply(g), between)
                if g == 0:
                    pe.wait_ge(ident_ready, 1)
                    pe.wait_ge(ones_ready, 2)
                    pe.wait_ge(weights_loaded, 64)
            for k in range(END, len(PIECES)):
                neighbor_part(k)


def kernel(x, adj, L0_gnn_num_neighbors, L0_gnn_fc_w, L0_gnn_fc_b):
    import concourse.bacc as _bacc
    from concourse.bass_utils import run_bass_kernel_spmd as _run

    x = np.ascontiguousarray(x)
    n, f = x.shape
    whole = n // P * P
    order = np.concatenate([np.arange(whole).reshape(P, whole // P).T.ravel(), np.arange(whole, n)])
    adj_t = np.asarray(adj)[order][:, order].T
    arrays = {"x": x}
    for g, (first, tiles, _) in enumerate(GROUPS):
        part = adj_t[:, first * P:(first + tiles) * P]
        arrays[f"adj_group{g}"] = np.ascontiguousarray(np.pad(part, ((0, 0), (0, -part.shape[1] % ALIGN))))
    arrays["num_neighbors"] = np.ascontiguousarray(L0_gnn_num_neighbors)
    arrays["fc_t"] = np.ascontiguousarray(np.asarray(L0_gnn_fc_w).T)
    arrays["fc_b"] = np.ascontiguousarray(L0_gnn_fc_b)
    nc = _bacc.Bacc("TRN2", target_bir_lowering=False, num_devices=1)
    ap = {k: nc.dram_tensor(k, v.shape, mybir.dt.from_np(v.dtype), kind="ExternalInput").ap() for k, v in arrays.items()}
    out = nc.dram_tensor("out", (n, f), F32, kind="ExternalOutput").ap()
    gnn_layer(nc, ap["x"], [ap[f"adj_group{g}"] for g in range(len(GROUPS))], ap["num_neighbors"], ap["fc_t"],
              ap["fc_b"], out)
    r = _run(nc, [arrays], core_ids=[0])
    return r.results[0]["out"]
```
